# Optimizing a Trainium2 kernel written in Bass

```python
import numpy as np
import jax
import jax.numpy as jnp

def _softmax(x, axis=-1):
    return jax.nn.softmax(x, axis=axis)

def _gelu(x):
    return jax.nn.gelu(x, approximate=True)

def _silu(x):
    return jax.nn.silu(x)

def _sigmoid(x):
    return jax.nn.sigmoid(x)

def _layernorm(x, axis=-1, eps=1e-05):
    m = jnp.mean(x, axis=axis, keepdims=True)
    v = jnp.var(x, axis=axis, keepdims=True)
    return (x - m) / jnp.sqrt(v + eps)

def _scatter_add(tgt, idx, src, axis=0):
    return tgt.at[idx].add(src)

def _segment_sum(src, seg, n):
    return jax.ops.segment_sum(src, seg, n)
kernel_name = 'mk_dlrm_tower_d1_rec_r8_8c864c'

def setup_inputs(seed: int=0):
    np.random.seed(seed)
    _w = jnp.asarray

    def _rec_inputs():
        import jax
        import jax.numpy as jnp
        _tk = jax.random.key(seed)
        dense_ctx = jax.random.normal(jax.random.fold_in(_tk, 190), (2048, 16), jnp.float32)
        ids = jnp.stack([jax.random.randint(jax.random.fold_in(_tk, 200 + f), (2048,), 0, v, jnp.int32) for f, v in enumerate([12500, 1000, 1250, 1000, 1000, 12500, 1000, 12500, 125000, 1000, 1250, 12500, 1250, 1250, 12500, 1000, 1250, 1250, 1250, 1000, 1000, 1000, 12500, 12500, 1250, 12500, 1250])], axis=1)
        tbl_0 = 0.05 * jax.random.normal(jax.random.fold_in(_tk, 500 + 0), (12500, 128), jnp.float32)
        tbl_1 = 0.05 * jax.random.normal(jax.random.fold_in(_tk, 500 + 1), (1000, 128), jnp.float32)
        tbl_2 = 0.05 * jax.random.normal(jax.random.fold_in(_tk, 500 + 2), (1250, 128), jnp.float32)
        tbl_3 = 0.05 * jax.random.normal(jax.random.fold_in(_tk, 500 + 3), (1000, 128), jnp.float32)
        tbl_4 = 0.05 * jax.random.normal(jax.random.fold_in(_tk, 500 + 4), (1000, 128), jnp.float32)
        tbl_5 = 0.05 * jax.random.normal(jax.random.fold_in(_tk, 500 + 5), (12500, 128), jnp.float32)
        tbl_6 = 0.05 * jax.random.normal(jax.random.fold_in(_tk, 500 + 6), (1000, 128), jnp.float32)
        tbl_7 = 0.05 * jax.random.normal(jax.random.fold_in(_tk, 500 + 7), (12500, 128), jnp.float32)
        tbl_8 = 0.05 * jax.random.normal(jax.random.fold_in(_tk, 500 + 8), (125000, 128), jnp.float32)
        tbl_9 = 0.05 * jax.random.normal(jax.random.fold_in(_tk, 500 + 9), (1000, 128), jnp.float32)
        tbl_10 = 0.05 * jax.random.normal(jax.random.fold_in(_tk, 500 + 10), (1250, 128), jnp.float32)
        tbl_11 = 0.05 * jax.random.normal(jax.random.fold_in(_tk, 500 + 11), (12500, 128), jnp.float32)
        tbl_12 = 0.05 * jax.random.normal(jax.random.fold_in(_tk, 500 + 12), (1250, 128), jnp.float32)
        tbl_13 = 0.05 * jax.random.normal(jax.random.fold_in(_tk, 500 + 13), (1250, 128), jnp.float32)
        tbl_14 = 0.05 * jax.random.normal(jax.random.fold_in(_tk, 500 + 14), (12500, 128), jnp.float32)
        tbl_15 = 0.05 * jax.random.normal(jax.random.fold_in(_tk, 500 + 15), (1000, 128), jnp.float32)
        tbl_16 = 0.05 * jax.random.normal(jax.random.fold_in(_tk, 500 + 16), (1250, 128), jnp.float32)
        tbl_17 = 0.05 * jax.random.normal(jax.random.fold_in(_tk, 500 + 17), (1250, 128), jnp.float32)
        tbl_18 = 0.05 * jax.random.normal(jax.random.fold_in(_tk, 500 + 18), (1250, 128), jnp.float32)
        tbl_19 = 0.05 * jax.random.normal(jax.random.fold_in(_tk, 500 + 19), (1000, 128), jnp.float32)
        tbl_20 = 0.05 * jax.random.normal(jax.random.fold_in(_tk, 500 + 20), (1000, 128), jnp.float32)
        tbl_21 = 0.05 * jax.random.normal(jax.random.fold_in(_tk, 500 + 21), (1000, 128), jnp.float32)
        tbl_22 = 0.05 * jax.random.normal(jax.random.fold_in(_tk, 500 + 22), (12500, 128), jnp.float32)
        tbl_23 = 0.05 * jax.random.normal(jax.random.fold_in(_tk, 500 + 23), (12500, 128), jnp.float32)
        tbl_24 = 0.05 * jax.random.normal(jax.random.fold_in(_tk, 500 + 24), (1250, 128), jnp.float32)
        tbl_25 = 0.05 * jax.random.normal(jax.random.fold_in(_tk, 500 + 25), (12500, 128), jnp.float32)
        tbl_26 = 0.05 * jax.random.normal(jax.random.fold_in(_tk, 500 + 26), (1250, 128), jnp.float32)
        _rk = jax.random.fold_in(_tk, 7)
        W_top1 = 0.0521996 * jax.random.normal(jax.random.fold_in(_tk, 801), (367, 512), jnp.float32)
        W_top2 = 0.0441942 * jax.random.normal(jax.random.fold_in(_tk, 802), (512, 256), jnp.float32)
        W_top3 = 0.0625 * jax.random.normal(jax.random.fold_in(_tk, 803), (256, 1), jnp.float32)
        b_top1 = jnp.zeros((512,), jnp.float32)
        b_top2 = jnp.zeros((256,), jnp.float32)
        return (dense_ctx, ids, tbl_0, tbl_1, tbl_2, tbl_3, tbl_4, tbl_5, tbl_6, tbl_7, tbl_8, tbl_9, tbl_10, tbl_11, tbl_12, tbl_13, tbl_14, tbl_15, tbl_16, tbl_17, tbl_18, tbl_19, tbl_20, tbl_21, tbl_22, tbl_23, tbl_24, tbl_25, tbl_26, W_top1, b_top1, W_top2, b_top2, W_top3)
    dense_ctx, ids, tbl_0, tbl_1, tbl_2, tbl_3, tbl_4, tbl_5, tbl_6, tbl_7, tbl_8, tbl_9, tbl_10, tbl_11, tbl_12, tbl_13, tbl_14, tbl_15, tbl_16, tbl_17, tbl_18, tbl_19, tbl_20, tbl_21, tbl_22, tbl_23, tbl_24, tbl_25, tbl_26, W_top1, b_top1, W_top2, b_top2, W_top3 = _rec_inputs()

    def _L0_rec_setup():
        import jax, jax.numpy as jnp
        import numpy as np

        def _tri_indices(num_feas):
            return np.array([i * num_feas + j for j in range(1, num_feas) for i in range(j)], dtype=np.int32)
        key = jax.random.key(seed)
        batch, num_feas, embed_dim = (2048, 27, 128)
        inputs = jax.random.normal(key, (batch, num_feas, embed_dim), dtype=jnp.float32)
        return {'inputs': inputs, 'num_feas': num_feas}
    _L0_rec_all = _L0_rec_setup()
    _L0_rec_in = {k: v for k, v in _L0_rec_all.items() if k in ()}
    del _L0_rec_all
    return {'dense_ctx': dense_ctx, 'ids': ids, 'tbl_0': tbl_0, 'tbl_1': tbl_1, 'tbl_2': tbl_2, 'tbl_3': tbl_3, 'tbl_4': tbl_4, 'tbl_5': tbl_5, 'tbl_6': tbl_6, 'tbl_7': tbl_7, 'tbl_8': tbl_8, 'tbl_9': tbl_9, 'tbl_10': tbl_10, 'tbl_11': tbl_11, 'tbl_12': tbl_12, 'tbl_13': tbl_13, 'tbl_14': tbl_14, 'tbl_15': tbl_15, 'tbl_16': tbl_16, 'tbl_17': tbl_17, 'tbl_18': tbl_18, 'tbl_19': tbl_19, 'tbl_20': tbl_20, 'tbl_21': tbl_21, 'tbl_22': tbl_22, 'tbl_23': tbl_23, 'tbl_24': tbl_24, 'tbl_25': tbl_25, 'tbl_26': tbl_26, 'W_top1': W_top1, 'b_top1': b_top1, 'W_top2': W_top2, 'b_top2': b_top2, 'W_top3': W_top3}

def reference(dense_ctx, ids, tbl_0, tbl_1, tbl_2, tbl_3, tbl_4, tbl_5, tbl_6, tbl_7, tbl_8, tbl_9, tbl_10, tbl_11, tbl_12, tbl_13, tbl_14, tbl_15, tbl_16, tbl_17, tbl_18, tbl_19, tbl_20, tbl_21, tbl_22, tbl_23, tbl_24, tbl_25, tbl_26, W_top1, b_top1, W_top2, b_top2, W_top3):
    import jax
    import jax.numpy as jnp

    def _L0_rec_ref(inputs, num_feas):
        import jax, jax.numpy as jnp
        import numpy as np

        def _tri_indices(num_feas):
            return np.array([i * num_feas + j for j in range(1, num_feas) for i in range(j)], dtype=np.int32)
        dot = jnp.einsum('bnd,bmd->bnm', inputs, inputs)
        idx = jnp.asarray(_tri_indices(num_feas))
        flat = dot.reshape(inputs.shape[0], num_feas * num_feas)
        return flat[:, idx]
    e = jnp.stack([tbl_0[ids[:, 0]], tbl_1[ids[:, 1]], tbl_2[ids[:, 2]], tbl_3[ids[:, 3]], tbl_4[ids[:, 4]], tbl_5[ids[:, 5]], tbl_6[ids[:, 6]], tbl_7[ids[:, 7]], tbl_8[ids[:, 8]], tbl_9[ids[:, 9]], tbl_10[ids[:, 10]], tbl_11[ids[:, 11]], tbl_12[ids[:, 12]], tbl_13[ids[:, 13]], tbl_14[ids[:, 14]], tbl_15[ids[:, 15]], tbl_16[ids[:, 16]], tbl_17[ids[:, 17]], tbl_18[ids[:, 18]], tbl_19[ids[:, 19]], tbl_20[ids[:, 20]], tbl_21[ids[:, 21]], tbl_22[ids[:, 22]], tbl_23[ids[:, 23]], tbl_24[ids[:, 24]], tbl_25[ids[:, 25]], tbl_26[ids[:, 26]]], axis=1)
    z = _L0_rec_ref(e, 27)
    z = z.reshape(z.shape[0], -1)
    h = jnp.concatenate([z, dense_ctx], axis=1)
    h = jnp.maximum(h @ W_top1 + b_top1, 0.0)
    h = jnp.maximum(h @ W_top2 + b_top2, 0.0)
    y = h @ W_top3
    return y

_drawn_inputs = setup_inputs


def setup_inputs(seed=0):
    import zlib

    import numpy as np

    out = dict(_drawn_inputs(seed))
    spreads = {'b_top1': (0.0, 0.1), 'b_top2': (0.0, 0.1)}
    factors = {}
    for name, (base, spread) in spreads.items():
        noise = np.random.default_rng([zlib.crc32(name.encode()), seed]).standard_normal(out[name].shape)
        drawn = base * np.exp(spread * noise) if base else spread * noise
        out[name] = jnp.asarray(drawn.astype(out[name].dtype))
    for name, factor in factors.items():
        out[name] = (out[name] * factor).astype(out[name].dtype)
    return out
```

```python
from contextlib import ExitStack

import concourse.bass as bass
from concourse import mybir

F32 = mybir.dt.float32
I32 = mybir.dt.int32
ALU = mybir.AluOpType
ACT = mybir.ActivationFunctionType

P = 128
BATCH = 2048
FEATS = 27
DIM = 128
DENSE = 16
HID1, HID2 = 512, 256
TILES = 4
COLS = TILES * P
GROUPS = BATCH // COLS
SLOTS = 2

FPB = 4
BANKS = [list(range(k, min(k + FPB, FEATS))) for k in range(0, FEATS, FPB)]
NB = len(BANKS)
SPM, MPU = 4, 4
QUAD = 32
RUN = COLS // SPM
UNITS = P // SPM // MPU
PJ = FEATS - 1

STARS = [(17, 10, 28), (9, 8, 16), (1, 8, 8)]
BASES = [0, 280, 408]
ZROWS = 472
ZLAST = ZROWS - 3 * P
DENSE_AT = 96
KROWS = [P, P, P, DENSE_AT + DENSE]
NZDMA = SPM * len(STARS)
M1, M2 = HID1 // P, HID2 // P
USE_L1 = list(range(1, 1 + M1))
USE_L2 = list(range(1 + M1, 1 + M1 + M2))
USE_L3 = 1 + M1 + M2
MLP_USES = USE_L3 + 1


def mlp_before(g, use):
    return MLP_USES // 2 * g + use // 2


def w1_pieces():
    for (j0, n, r), base in zip(STARS, BASES):
        for j in range(j0, j0 + n):
            row, left, src = base + (j - j0) * r, j, j * (j - 1) // 2
            while left:
                m = min(left, P - row % P)
                yield row, src, m
                row, left, src = row + m, left - m, src + m
    yield 3 * P + DENSE_AT, FEATS * PJ // 2, DENSE


W1_LOADS = len(list(w1_pieces()))


def wait_if(eng, sem, value):
    if isinstance(value, int) and value <= 0:
        return
    eng.wait_ge(sem, value)


def dlrm(nc, inp, z_dram, y_dram):
    with ExitStack() as ctx:
        def sb(name, shape, dt=F32):
            return ctx.enter_context(nc.sbuf_tensor(name, shape, dt))

        def bank(name):
            return ctx.enter_context(nc.psum_tensor(name, [P, 512], F32))

        def sem(name):
            return ctx.enter_context(nc.semaphore(name))

        ids = sb("ids", [P, TILES, FEATS], I32)
        rows = [sb(f"rows{s}", [P, FEATS, DIM]) for s in range(SLOTS)]
        embT = [sb(f"embT{s}", [P, P, QUAD]) for s in range(SLOTS)]
        dots = sb("dots", [P, PJ, RUN])
        zT = sb("zT", [P, len(KROWS), COLS])
        h1T = sb("h1T", [P, M1, COLS])
        h2T = sb("h2T", [P, M2, COLS])
        y = sb("y", [1, COLS])
        ident = sb("ident", [P, P])
        dense = sb("dense", [P, TILES, DENSE])
        w1 = sb("w1", [P, len(KROWS), HID1])
        w2 = sb("w2", [P, M1, HID2])
        w3 = sb("w3", [P, M2])
        b1 = sb("b1", [P, M1])
        b2 = sb("b2", [P, M2])

        ps_turn = [bank(f"ps_turn{i}") for i in range(2)]
        ps_dot = [bank(f"ps_dot{i}") for i in range(2)]
        ps_mlp = [bank(f"ps_mlp{i}") for i in range(2)]

        ids_loaded = [sem(f"ids_loaded{t}") for t in range(TILES)]
        gathered = [[sem(f"gathered{s}_{k}") for k in range(NB)] for s in range(SLOTS)]
        turned = [sem(f"turned{i}") for i in range(2)]
        turn_taken = [sem(f"turn_taken{i}") for i in range(2)]
        dotted = [sem(f"dotted{i}") for i in range(2)]
        dot_taken = [sem(f"dot_taken{i}") for i in range(2)]
        z_stored = sem("z_stored")
        z_loaded = sem("z_loaded")
        dense_loaded = sem("dense_loaded")
        dense_turned = sem("dense_turned")
        l1_done = sem("l1_done")
        l2_done = sem("l2_done")
        l3_done = sem("l3_done")
        y_stored = sem("y_stored")
        rows_free = sem("rows_free")
        y_seen = sem("y_seen")
        mlp_taken = [sem(f"mlp_taken{i}") for i in range(2)]
        ident_zero = sem("ident_zero")
        ident_ready = sem("ident_ready")
        w1_zero = sem("w1_zero")
        tails_zero = sem("tails_zero")
        w1_loaded = sem("w1_loaded")
        w2_loaded = sem("w2_loaded")
        w3_loaded = sem("w3_loaded")
        bias_loaded = sem("bias_loaded")

        ids_v = inp["ids"].rearrange("(g p t) f -> g p t f", p=P, t=TILES)
        dense_v = inp["dense_ctx"].rearrange("(g p t) k -> g p t k", p=P, t=TILES)

        def turn_use(t, k):
            return NB * t + k

        def turns_before(g, t, k):
            return g * (NB * TILES // 2) + turn_use(t, k) // 2

        def turns_of(g, t, half):
            return g * (NB * TILES // 2) + (turn_use(t, NB - 1) - half) // 2 + 1

        def dots_until(g, t):
            return (g * TILES + t) * (UNITS // 2)

        block = ctx.enter_context(nc.Block())

        @block.gpsimd
        def _(pool):
            nc.gpsimd.memset(ident[:, :], 0.0).then_inc(ident_zero, 1)
            pool.wait_ge(ident_zero, 1)
            nc.gpsimd.affine_select(out=ident[:, :], in_=ident[:, :], compare_op=ALU.not_equal, fill=1.0,
                                    base=0, pattern=[[-1, P]], channel_multiplier=1).then_inc(ident_ready, 1)

            def gather_group(g):
                for t in range(TILES):
                    slot = t % SLOTS
                    pool.wait_ge(ids_loaded[t], 16 * (g + 1))
                    for k, feats in enumerate(BANKS):
                        if t >= SLOTS or not isinstance(g, int):
                            pool.wait_ge(turned[turn_use(t - SLOTS, k) % 2],
                                         turns_before(g, t - SLOTS, k) + 1)
                            pool.sem_inc(rows_free, 1)
                        for f in feats:
                            nc.gpsimd.indirect_dma_start(
                                rows[slot][:, f, :], None, inp[f"tbl_{f}"],
                                bass.IndirectOffsetOnAxis(ap=ids[:, t, f:f + 1], axis=0),
                            ).then_inc(gathered[slot][k], 16)

            gather_group(0)
            with pool.Fori(1, GROUPS) as g:
                gather_group(g)

        @block.sync
        def _(sp):
            def load_ids(g, t):
                sp.dma_start(ids[:, t, :], ids_v[g, :, t, :]).then_inc(ids_loaded[t], 16)

            def load_dense(g):
                wait_if(sp, dense_turned, g)
                sp.dma_start(dense[:, :, :], dense_v[g]).then_inc(dense_loaded, 16)

            def bounce(g):
                for i in range(2):
                    sp.wait_ge(dot_taken[i], dots_until(g, TILES))
                for s in range(SPM):
                    for (j0, n, r), base in zip(STARS, BASES):
                        dst = z_dram[g, base:base + n * r, s * RUN:(s + 1) * RUN]
                        sp.dma_start(dst.rearrange("(j i) c -> i j c", i=r),
                                     dots[s * QUAD:s * QUAD + r, j0 - 1:j0 - 1 + n, :]).then_inc(z_stored, 16)
                sp.wait_ge(z_stored, 16 * NZDMA * (g + 1))
                wait_if(sp, l1_done, M1 * g)
                sp.dma_start(zT[:, 0:3, :], z_dram[g, 0:3 * P, :].rearrange("(c p) b -> p c b", p=P)).then_inc(z_loaded, 16)
                sp.dma_start(zT[0:ZLAST, 3, :], z_dram[g, 3 * P:ZROWS, :]).then_inc(z_loaded, 16)

            def store_y(g):
                sp.wait_ge(mlp_taken[USE_L3 % 2], mlp_before(g, USE_L3) + 1)
                sp.sem_inc(y_seen, 1)
                sp.dma_start(y_dram[bass.ds(g, 1), :], y[:, :]).then_inc(y_stored, 16)

            def refill_ids(g):
                for t in range(TILES):
                    sp.wait_ge(turned[turn_use(t, NB - 1) % 2], turns_before(g, t, NB - 1) + 1)
                    load_ids(g + 1, t)

            for t in range(TILES):
                load_ids(0, t)
            load_dense(0)
            refill_ids(0)
            bounce(0)
            with sp.Fori(1, GROUPS - 1) as g:
                refill_ids(g)
                load_dense(g)
                store_y(g - 1)
                bounce(g)
            load_dense(GROUPS - 1)
            store_y(GROUPS - 2)
            bounce(GROUPS - 1)
            store_y(GROUPS - 1)
            sp.wait_ge(y_stored, 16 * GROUPS)

        def transposes_taken(eng, copy, half, g, t):
            slot = t % SLOTS
            dst = embT[slot][:, :, :].rearrange("d p f -> d f p")
            for k, feats in enumerate(BANKS):
                if turn_use(t, k) % 2 != half:
                    continue
                eng.wait_ge(turned[half], turns_before(g, t, k) + 1)
                if t >= SLOTS or not isinstance(g, int):
                    for i in range(2):
                        eng.wait_ge(dotted[i], dots_until(g, t - SLOTS + 1))
                n = len(feats)
                copy(dst[:, feats[0]:feats[0] + n, :],
                     ps_turn[half][:, 0:n * P].rearrange("d (f p) -> d f p", f=n)).then_inc(turn_taken[half], 1)

        def dots_taken(eng, copy, half, g, t):
            if t == 0:
                wait_if(eng, z_stored, 16 * NZDMA * g)
            for u in range(half, UNITS, 2):
                eng.wait_ge(dotted[half], dots_until(g, t) + u // 2 + 1)
                src = ps_dot[half][:, :].rearrange("p (q c) -> p q c", q=MPU)
                for s in range(SPM):
                    out = dots[s * QUAD:(s + 1) * QUAD, :, :].rearrange("p j (q t) -> p q j t", t=TILES)
                    last = copy(out[:, u * MPU:(u + 1) * MPU, :, t],
                                src[s * QUAD:(s + 1) * QUAD, :, s * PJ:(s + 1) * PJ])
                last.then_inc(dot_taken[half], 1)

        @block.scalar
        def _(act):
            act.wait_ge(w1_zero, 1)
            for row, src, n in w1_pieces():
                act.dma_start(w1[row % P:row % P + n, row // P, :], inp["W_top1"][src:src + n, :]).then_inc(w1_loaded, 16)
            act.dma_start(w2[:, :, :], inp["W_top2"].rearrange("(k p) n -> p k n", p=P)).then_inc(w2_loaded, 16)
            for m in range(M1):
                act.dma_start(b1[:, m:m + 1], inp["b_top1"][m * P:(m + 1) * P].rearrange("(p o) -> p o", o=1)).then_inc(bias_loaded, 16)
            for m in range(M2):
                act.dma_start(b2[:, m:m + 1], inp["b_top2"][m * P:(m + 1) * P].rearrange("(p o) -> p o", o=1)).then_inc(bias_loaded, 16)
                act.dma_start(w3[:, m:m + 1], inp["W_top3"][m * P:(m + 1) * P, :]).then_inc(w3_loaded, 16)
            act.wait_ge(bias_loaded, 16 * (M1 + M2))

            def layer1(g, ms):
                for m in ms:
                    half = USE_L1[m] % 2
                    act.wait_ge(l1_done, M1 * g + m + 1)
                    if m == 0:
                        wait_if(act, l2_done, M2 * g)
                    nc.scalar.activation(h1T[:, m, :], ps_mlp[half][:, :], ACT.Relu,
                                         bias=b1[:, m:m + 1]).then_inc(mlp_taken[half], 1)

            def layer2(g):
                for m in range(M2):
                    half = USE_L2[m] % 2
                    act.wait_ge(l2_done, M2 * g + m + 1)
                    if m == 0:
                        wait_if(act, l3_done, g)
                    nc.scalar.activation(h2T[:, m, :], ps_mlp[half][:, :], ACT.Relu,
                                         bias=b2[:, m:m + 1]).then_inc(mlp_taken[half], 1)

            def tile(g, t):
                transposes_taken(act, nc.scalar.copy, 0, g, t)
                dots_taken(act, nc.scalar.copy, 0, g, t)

            for t in range(TILES):
                tile(0, t)
            with act.Fori(1, GROUPS) as g:
                tile(g, 0)
                layer1(g - 1, [0, 1])
                tile(g, 1)
                layer1(g - 1, [2, 3])
                tile(g, 2)
                layer2(g - 1)
                tile(g, 3)
            layer1(GROUPS - 1, range(M1))
            layer2(GROUPS - 1)

        @block.vector
        def _(dve):
            nc.vector.memset(w1[:, :, :], 0.0).then_inc(w1_zero, 1)
            for s in range(SLOTS):
                nc.vector.memset(embT[s][:, :, FEATS:], 0.0).then_inc(tails_zero, 1)
            nc.vector.memset(zT[ZLAST // QUAD * QUAD:P, 3, :], 0.0).then_inc(tails_zero, 1)

            def take_dense(g):
                dve.wait_ge(dense_turned, g + 1)
                wait_if(dve, l1_done, M1 * g)
                nc.vector.tensor_copy(zT[DENSE_AT:DENSE_AT + DENSE, 3, :].rearrange("k (s q t) -> k t q s", s=SPM, t=TILES),
                                      ps_mlp[0][0:DENSE, :].rearrange("k (t q s) -> k t q s", t=TILES, s=SPM)).then_inc(mlp_taken[0], 1)

            def take_y(g):
                dve.wait_ge(l3_done, g + 1)
                wait_if(dve, y_stored, 16 * g)
                nc.vector.tensor_copy(y[:, :].rearrange("o (q s t) -> o s q t", s=SPM, t=TILES),
                                      ps_mlp[1][0:1, :].rearrange("o (s q t) -> o s q t", s=SPM, t=TILES)).then_inc(mlp_taken[1], 1)

            def tile(g, t):
                transposes_taken(dve, nc.vector.tensor_copy, 1, g, t)
                dots_taken(dve, nc.vector.tensor_copy, 1, g, t)

            for t in range(TILES):
                tile(0, t)
            with dve.Fori(1, GROUPS) as g:
                tile(g, 0)
                take_dense(g - 1)
                tile(g, 1)
                tile(g, 2)
                tile(g, 3)
                take_y(g - 1)
            take_dense(GROUPS - 1)
            take_y(GROUPS - 1)

        @block.tensor
        def _(pe):
            def turn(g, t):
                slot = t % SLOTS
                for k, feats in enumerate(BANKS):
                    half = turn_use(t, k) % 2
                    pe.wait_ge(gathered[slot][k], 16 * len(feats) * (g * (TILES // SLOTS) + t // SLOTS + 1))
                    wait_if(pe, turn_taken[half], turns_before(g, t, k))
                    for i, f in enumerate(feats):
                        last = nc.tensor.transpose(ps_turn[half][:, i * P:(i + 1) * P], rows[slot][:, f, :], ident[:, :])
                    last.then_inc(turned[half], 1)

            def dot(g, t):
                slot = t % SLOTS
                for half in range(2):
                    pe.wait_ge(turn_taken[half], turns_of(g, t, half))
                for u in range(UNITS):
                    wait_if(pe, dot_taken[u % 2], dots_until(g, t) + u // 2)
                    for m in range(MPU):
                        q = u * MPU + m
                        left = embT[slot][:, q * SPM:(q + 1) * SPM, :].rearrange("d s f -> d (s f)")
                        right = embT[slot][:, q * SPM:(q + 1) * SPM, 1:FEATS]
                        last = nc.tensor.matmul(ps_dot[u % 2][:, m * P:m * P + SPM * PJ], left, right, start=True, stop=True)
                    last.then_inc(dotted[u % 2], 1)

            def turn_dense(g):
                pe.wait_ge(dense_loaded, 16 * (g + 1))
                wait_if(pe, mlp_taken[0], mlp_before(g, 0))
                for t in range(TILES):
                    last = nc.tensor.transpose(ps_mlp[0][0:DENSE, t * P:(t + 1) * P], dense[:, t, :], ident[:, :])
                last.then_inc(dense_turned, 1)

            def layer1(g, ms):
                if 0 in ms:
                    pe.wait_ge(z_loaded, 32 * (g + 1))
                    pe.wait_ge(mlp_taken[0], mlp_before(g, 0) + 1)
                for m in ms:
                    half = USE_L1[m] % 2
                    wait_if(pe, mlp_taken[half], mlp_before(g, USE_L1[m]))
                    for c, k in enumerate(KROWS):
                        last = nc.tensor.matmul(ps_mlp[half][:, :], w1[0:k, c, m * P:(m + 1) * P], zT[0:k, c, :],
                                                start=(c == 0), stop=(c == len(KROWS) - 1))
                    last.then_inc(l1_done, 1)

            def layer2(g):
                for use in USE_L1[-2:]:
                    pe.wait_ge(mlp_taken[use % 2], mlp_before(g, use) + 1)
                for m in range(M2):
                    half = USE_L2[m] % 2
                    wait_if(pe, mlp_taken[half], mlp_before(g, USE_L2[m]))
                    for c in range(M1):
                        last = nc.tensor.matmul(ps_mlp[half][:, :], w2[:, c, m * P:(m + 1) * P], h1T[:, c, :],
                                                start=(c == 0), stop=(c == M1 - 1))
                    last.then_inc(l2_done, 1)

            def layer3(g):
                for use in USE_L2:
                    pe.wait_ge(mlp_taken[use % 2], mlp_before(g, use) + 1)
                for c in range(M2):
                    last = nc.tensor.matmul(ps_mlp[USE_L3 % 2][0:1, :], w3[:, c:c + 1], h2T[:, c, :],
                                            start=(c == 0), stop=(c == M2 - 1))
                last.then_inc(l3_done, 1)

            def tile(g, t):
                turn(g, t)
                dot(g, t)

            pe.wait_ge(ident_ready, 1)
            pe.wait_ge(tails_zero, SLOTS + 1)
            for t in range(TILES):
                tile(0, t)
            pe.wait_ge(w1_loaded, 16 * W1_LOADS)
            pe.wait_ge(w2_loaded, 16)
            pe.wait_ge(w3_loaded, 16 * M2)
            with pe.Fori(1, GROUPS) as g:
                tile(g, 0)
                turn_dense(g - 1)
                layer1(g - 1, [0, 1])
                tile(g, 1)
                layer1(g - 1, [2, 3])
                tile(g, 2)
                layer2(g - 1)
                tile(g, 3)
                layer3(g - 1)
            turn_dense(GROUPS - 1)
            layer1(GROUPS - 1, range(M1))
            layer2(GROUPS - 1)
            layer3(GROUPS - 1)


_INS = ["dense_ctx", "ids"] + [f"tbl_{f}" for f in range(FEATS)] + ["W_top1", "b_top1", "W_top2", "b_top2", "W_top3"]


def kernel(**inputs):
    import numpy as _np
    import concourse.bacc as _bacc
    from concourse import mybir as _mybir
    from concourse.bass_utils import run_bass_kernel_spmd as _run

    nc = _bacc.Bacc("TRN2", target_bir_lowering=False, num_devices=1)
    arrays, aps = {}, {}
    for name in _INS:
        a = _np.ascontiguousarray(inputs[name])
        arrays[f"in_{name}_dram"] = a
        aps[name] = nc.dram_tensor(f"in_{name}_dram", a.shape, _mybir.dt.from_np(a.dtype), kind="ExternalInput").ap()
    z = nc.dram_tensor("z_dram", (GROUPS, ZROWS, COLS), _mybir.dt.float32).ap()
    y = nc.dram_tensor("out_0_dram", (BATCH, 1), _mybir.dt.float32, kind="ExternalOutput").ap()
    dlrm(nc, aps, z, y.rearrange("(g c) o -> g (c o)", g=GROUPS))
    r = _run(nc, [arrays], core_ids=[0])
    return r.results[0]["out_0_dram"]
```

```python
from contextlib import ExitStack

import concourse.bass as bass
from concourse import mybir

F32 = mybir.dt.float32
F16 = mybir.dt.float16
F32R = mybir.dt.float32r
U32 = mybir.dt.uint32
I32 = mybir.dt.int32
ALU = mybir.AluOpType
ACT = mybir.ActivationFunctionType

P = 128
BATCH = 2048
FEATS = 27
DIM = 128
DENSE = 16
HID1, HID2 = 512, 256
TILES = 2
COLS = TILES * P
PAIRS = BATCH // COLS

ONEHOT = [[3, 4], [9, 15], [19, 20], [6, 21]]
STEPS = len(ONEHOT)
TABLES = [range(2 * i, 2 * i + len(step)) for i, step in enumerate(ONEHOT)]
LAST_TABLES = [step[-1] for step in TABLES]
OH_FEATS = [f for step in ONEHOT for f in step]
OH_ROWS = 1000
CHUNKS = 8
OH_P = OH_ROWS // CHUNKS
PARTS = 2
HIGH_MASK = 0xFFFFF000
BUFS = 4

GATHERED = [f for f in range(FEATS) if f not in OH_FEATS]
NG = len(GATHERED)
FPB = 4
BANKS = [GATHERED[k:k + FPB] for k in range(0, NG, FPB)]
NB = len(BANKS)

SPM, MPU = 4, 4
GROUPS = P // SPM
UNITS = GROUPS // MPU
RUN = TILES * GROUPS
I_ROWS = FEATS - 1
M_DOT = (SPM - 1) * FEATS + I_ROWS
PJ = FEATS - 1

BLOCKS = [[26, 24, 14], [22, 20, 16, 6], [18, 12, 10, 8, 4, 2]]
FIRST = [0, 0, DENSE]
DENSE_CHUNK = len(FIRST) - 1
POOL_CHUNK = 1
KROWS = [first + sum(2 * r for r in chunk) for first, chunk in zip(FIRST, BLOCKS)]
Z_PLACES = [(r, c, FIRST[c] + sum(2 * x for x in chunk[:n]))
            for c, chunk in enumerate(BLOCKS) for n, r in enumerate(chunk)]
assert max(KROWS) <= P and sorted(r for r, _, _ in Z_PLACES) == list(range(2, FEATS, 2))
M1, M2 = HID1 // P, HID2 // P
USE_L1 = list(range(1, 1 + M1))
USE_L2 = list(range(1 + M1, 1 + M1 + M2))
USE_L3 = 1 + M1 + M2
MLP_USES = USE_L3 + 1
W1_LOADS = 2 * len(Z_PLACES) + 1


def runs(feats):
    out = []
    for i, f in enumerate(feats):
        if out and f == out[-1][1] + out[-1][2]:
            out[-1][2] += 1
        else:
            out.append([i, f, 1])
    return out


def mlp_before(n, use):
    return MLP_USES // 2 * n + use // 2


def turn_half(t, k):
    return (NB * t + k) % 2


def turns_before(j, t, k):
    return NB * j + (NB * t + k) // 2


def turns_of(j, t, half):
    return NB * j + (NB * (t + 1) - 1 - half) // 2 + 1


def dots_until(j, t):
    return TILES * (UNITS // 2) * j + UNITS // 2 * t


def before_in_buffer(x):
    return x - BUFS if x >= BUFS else max(range(x, len(OH_FEATS), BUFS)) - len(OH_FEATS)


def wait_if(eng, sem, value):
    if isinstance(value, int) and value <= 0:
        return
    eng.wait_ge(sem, value)


def dlrm(nc, inp, z_dram, y_dram):
    with ExitStack() as ctx:
        def sb(name, shape, dt=F32):
            return ctx.enter_context(nc.sbuf_tensor(name, shape, dt))

        def bank(name):
            return ctx.enter_context(nc.psum_tensor(name, [P, 512], F32))

        def sem(name):
            return ctx.enter_context(nc.semaphore(name))

        ids = sb("ids", [P, TILES, FEATS], I32)
        ids_all = sb("ids_all", [P, PAIRS, TILES * FEATS], I32)
        ids16 = sb("ids16", [P, PAIRS, TILES * FEATS], F16)
        rows = [sb(f"rows{t}", [P, NG, DIM]) for t in range(TILES)]
        embT = sb("embT", [P, TILES, P, FEATS])
        table = [sb(f"table{x}", [P, CHUNKS, PARTS, DIM], F32R) for x in range(len(OH_FEATS))]
        row_ids = sb("row_ids", [P, CHUNKS], I32)
        row_idsf = sb("row_idsf", [P, CHUNKS])
        spread = [sb(f"spread{i}", [P, 2, COLS], F16) for i in range(STEPS)]
        onehot = [sb(f"onehot{i}", [P, CHUNKS, COLS], F32R) for i in range(BUFS)]
        dots = sb("dots", [P, SPM * PJ, RUN])
        span = CHUNKS * DIM // RUN
        spans = [dots[:, i * span:(i + 1) * span, :].rearrange("p a b -> p (a b)")
                 .rearrange("p (c d) -> p c d", d=DIM) for i in range(SPM * PJ // span)]
        raw, high = spans[0:4], spans[4:6]
        zT = sb("zT", [P, len(KROWS), COLS])
        z_lastT = rows[0][:, 0:len(KROWS) * COLS // DIM, :].rearrange("p a d -> p (a d)").rearrange("p (k c) -> p k c", c=COLS)
        h1T = sb("h1T", [P, M1, COLS])
        h2T = sb("h2T", [P, M2, COLS])
        y = sb("y", [1, BATCH])
        ident = sb("ident", [P, P])
        ident16 = sb("ident16", [P, P], F16)
        dense = sb("dense", [P, TILES, DENSE])
        w1 = sb("w1", [P, len(KROWS), HID1])
        w2 = sb("w2", [P, M1, HID2])
        w3 = sb("w3", [P, M2])
        b1 = sb("b1", [P, M1])
        b2 = sb("b2", [P, M2])

        ps_turn = [bank(f"ps_turn{i}") for i in range(2)]
        ps_dot = [bank(f"ps_dot{i}") for i in range(2)]
        ps_mlp = [bank(f"ps_mlp{i}") for i in range(2)]
        ps_spread = bank("ps_spread")
        ps_pick = bank("ps_pick")

        ids_loaded = [sem(f"ids_loaded{t}") for t in range(TILES)]
        ids_all_loaded = sem("ids_all_loaded")
        ids16_ready = sem("ids16_ready")
        rows_free = sem("rows_free")
        gathered = [[sem(f"gathered{t}_{k}") for k in range(NB)] for t in range(TILES)]
        turned = [sem(f"turned{i}") for i in range(2)]
        turn_taken = [sem(f"turn_taken{i}") for i in range(2)]
        raw_loaded = [sem(f"raw_loaded{x}") for x in range(len(OH_FEATS))]
        masked = sem("masked")
        high_ready = sem("high_ready")
        low_ready = sem("low_ready")
        table_done = sem("table_done")
        spread_done = sem("spread_done")
        spread_taken = sem("spread_taken")
        onehot_ready = sem("onehot_ready")
        pick_taken = sem("pick_taken")
        dotted = [sem(f"dotted{i}") for i in range(2)]
        dot_taken = [sem(f"dot_taken{i}") for i in range(2)]
        z_stored = sem("z_stored")
        z_loaded = sem("z_loaded")
        z_last_loaded = [sem(f"z_last_loaded{c}") for c in range(len(KROWS))]
        dense_loaded = sem("dense_loaded")
        dense_turned = sem("dense_turned")
        l1_done = sem("l1_done")
        l2_done = sem("l2_done")
        l3_done = sem("l3_done")
        mlp_taken = [sem(f"mlp_taken{i}") for i in range(2)]
        y_stored = sem("y_stored")
        ident_zero = sem("ident_zero")
        ident_ready = sem("ident_ready")
        ident16_ready = sem("ident16_ready")
        row_ids_made = sem("row_ids_made")
        row_ids_ready = sem("row_ids_ready")
        w1_zero = sem("w1_zero")
        w1_loaded = sem("w1_loaded")
        w2_loaded = sem("w2_loaded")
        w3_loaded = sem("w3_loaded")
        bias_loaded = sem("bias_loaded")

        ids_v = inp["ids"].rearrange("(j p t) f -> j p t f", p=P, t=TILES)
        dense_v = inp["dense_ctx"].rearrange("(j p t) k -> j p t k", p=P, t=TILES)

        LAST_BANKS = [*ps_turn, ps_spread, ps_pick]

        def dots_of(s):
            return dots[s * FEATS:s * FEATS + I_ROWS, s * PJ:(s + 1) * PJ, :]

        def z_view(j):
            return z_dram[j].rearrange("(j i c) -> i j c", i=I_ROWS, c=COLS)

        def load_last(eng, chunks):
            for r, c, at in Z_PLACES:
                if c in chunks:
                    eng.dma_start(z_lastT[at:at + 2 * r, c, :], z_view(PAIRS - 1)[0:r, r - 2:r, :],
                                  ).then_inc(z_last_loaded[c], 16)

        block = ctx.enter_context(nc.Block())

        @block.gpsimd
        def _(pool):
            nc.gpsimd.memset(ident[:, :], 0.0).then_inc(ident_zero, 1)
            pool.wait_ge(ident_zero, 1)
            nc.gpsimd.affine_select(out=ident[:, :], in_=ident[:, :], compare_op=ALU.not_equal, fill=1.0,
                                    base=0, pattern=[[-1, P]], channel_multiplier=1).then_inc(ident_ready, 1)
            nc.gpsimd.iota(row_ids[:, :], pattern=[[1, CHUNKS]], base=0,
                           channel_multiplier=CHUNKS).then_inc(row_ids_made, 1)
            nc.gpsimd.memset(w1[:, :, :], 0.0).then_inc(w1_zero, 1)

            def gather_pair(j):
                for t in range(TILES):
                    pool.wait_ge(ids_loaded[t], 16 * (j + 1))
                    for k, feats in enumerate(BANKS):
                        if not isinstance(j, int):
                            pool.wait_ge(turned[turn_half(t, k)], turns_before(j - 1, t, k) + 1)
                            pool.sem_inc(rows_free, 1)
                        for f in feats:
                            nc.gpsimd.indirect_dma_start(
                                rows[t][:, GATHERED.index(f), :], None, inp[f"tbl_{f}"],
                                bass.IndirectOffsetOnAxis(ap=ids[:, t, f:f + 1], axis=0),
                            ).then_inc(gathered[t][k], 16)

            gather_pair(0)
            with pool.Fori(1, PAIRS) as j:
                gather_pair(j)
            pool.wait_ge(z_stored, 16 * SPM * (PAIRS - 1 + TILES))
            load_last(nc.gpsimd, [POOL_CHUNK])

        @block.sync
        def _(sp):
            def load_ids(j, t):
                sp.dma_start(ids[:, t, :], ids_v[j, :, t, :]).then_inc(ids_loaded[t], 16)

            def load_dense(j):
                wait_if(sp, dense_turned, j)
                sp.dma_start(dense[:, :, :], dense_v[j]).then_inc(dense_loaded, 16)

            def refill_ids(j):
                for t in range(TILES):
                    sp.wait_ge(turned[turn_half(t, NB - 1)], turns_before(j, t, NB - 1) + 1)
                    load_ids(j + 1, t)

            def bounce(j):
                for i in range(2):
                    sp.wait_ge(dot_taken[i], dots_until(j, TILES))
                z = z_view(j)
                for s in range(SPM):
                    sp.dma_start(z[:, :, s * RUN:(s + 1) * RUN],
                                 dots_of(s)[:, :, :]).then_inc(z_stored, 16)
                sp.wait_ge(z_stored, 16 * SPM * (j + 1))
                for r, c, at in Z_PLACES:
                    sp.dma_start(zT[at:at + 2 * r, c, :], z[0:r, r - 2:r, :]).then_inc(z_loaded, 16)

            def bounce_last():
                z = z_view(PAIRS - 1)
                for t in range(TILES):
                    for i in range(2):
                        sp.wait_ge(dot_taken[i], dots_until(PAIRS - 1, t + 1))
                    for s in range(SPM):
                        at = s * RUN + t * GROUPS
                        sp.dma_start(z[:, :, at:at + GROUPS], dots_of(s)[:, :, t * GROUPS:(t + 1) * GROUPS],
                                     ).then_inc(z_stored, 16)
                sp.wait_ge(z_stored, 16 * SPM * (PAIRS - 1 + TILES))
                load_last(nc.sync, [c for c in range(len(KROWS)) if c != POOL_CHUNK])

            for t in range(TILES):
                load_ids(0, t)
            sp.dma_start(ids_all[:, :, :], inp["ids"].rearrange("(j p t) f -> p j (t f)", p=P, t=TILES)).then_inc(ids_all_loaded, 16)
            for x, f in enumerate(OH_FEATS):
                if x >= len(raw):
                    sp.wait_ge(low_ready, x - len(raw) + 1)
                sp.dma_start(raw[x % len(raw)][0:OH_P, :, :],
                             inp[f"tbl_{f}"].rearrange("(p c) d -> p c d", c=CHUNKS)).then_inc(raw_loaded[x], 16)
                if x == 3:
                    load_dense(0)
            sp.wait_ge(w1_zero, 1)
            for r, c, at in Z_PLACES:
                for j in (r - 1, r):
                    first = at + j - (r - 1)
                    sp.dma_start(w1[first:first + 2 * j - 1:2, c, :],
                                 inp["W_top1"][j * (j - 1) // 2:j * (j - 1) // 2 + j, :]).then_inc(w1_loaded, 16)
            sp.dma_start(w1[0:DENSE, DENSE_CHUNK, :], inp["W_top1"][FEATS * PJ // 2:, :]).then_inc(w1_loaded, 16)
            sp.dma_start(w2[:, :, :], inp["W_top2"].rearrange("(k p) n -> p k n", p=P)).then_inc(w2_loaded, 16)
            for m in range(M1):
                sp.dma_start(b1[:, m:m + 1], inp["b_top1"][m * P:(m + 1) * P].rearrange("(p o) -> p o", o=1)).then_inc(bias_loaded, 16)
            for m in range(M2):
                sp.dma_start(b2[:, m:m + 1], inp["b_top2"][m * P:(m + 1) * P].rearrange("(p o) -> p o", o=1)).then_inc(bias_loaded, 16)
                sp.dma_start(w3[:, m:m + 1], inp["W_top3"][m * P:(m + 1) * P, :]).then_inc(w3_loaded, 16)

            refill_ids(0)
            bounce(0)
            with sp.Fori(1, PAIRS - 1) as j:
                refill_ids(j)
                load_dense(j)
                bounce(j)
            load_dense(PAIRS - 1)
            bounce_last()
            sp.wait_ge(mlp_taken[USE_L3 % 2], mlp_before(PAIRS - 1, USE_L3) + 1)
            sp.dma_start(y_dram, y[:, :]).then_inc(y_stored, 16)
            sp.wait_ge(y_stored, 16)

        def take_turned(eng, copy, j, t, k):
            half = turn_half(t, k)
            eng.wait_ge(turned[half], turns_before(j, t, k) + 1)
            for at, f, n in runs(BANKS[k]):
                last = copy(embT[:, t, :, f:f + n].rearrange("d p f -> d f p"),
                            ps_turn[half][:, at * P:(at + n) * P].rearrange("d (f p) -> d f p", f=n))
            last.then_inc(turn_taken[half], 1)

        def take_dots(eng, copy, j, t, u):
            half = u % 2
            if t == 0 and u < 2:
                wait_if(eng, z_stored, 16 * SPM * j)
            eng.wait_ge(dotted[half], dots_until(j, t) + u // 2 + 1)
            first = t * GROUPS + u * MPU
            last = copy(dots[0:M_DOT, :, first:first + MPU].rearrange("p c q -> p q c"),
                        ps_dot[half][0:M_DOT, :].rearrange("p (q c) -> p q c", q=MPU)[:, :, 0:SPM * PJ])
            last.then_inc(dot_taken[half], 1)

        @block.scalar
        def _(act):
            def take_spread(j, step):
                act.wait_ge(spread_done, STEPS * j + step + 1)
                n = len(ONEHOT[step])
                nc.scalar.copy(spread[step][:, 0:n, :],
                               ps_spread[:, 0:n * COLS].rearrange("p (x c) -> p x c", x=n)).then_inc(spread_taken, 1)

            def take_picked(j, step):
                act.wait_ge(table_done, len(OH_FEATS) * j + LAST_TABLES[step] + 1)
                feats = ONEHOT[step]
                n = len(feats)
                by = feats[-1] - feats[0] if n > 1 else 1
                for t in range(TILES):
                    last = nc.scalar.copy(
                        embT[:, t, :, feats[0]:feats[-1] + 1:by].rearrange("d p f -> d f p"),
                        ps_pick[:, 0:n * COLS].rearrange("d (f t p) -> d t f p", f=n, t=TILES)[:, t, :, :])
                last.then_inc(pick_taken, 1)

            def layer1(n, m, src=None):
                half = USE_L1[m] % 2
                act.wait_ge(l1_done, M1 * n + m + 1)
                nc.scalar.activation(h1T[:, m, :], (src or ps_mlp[half])[:, 0:COLS], ACT.Relu,
                                     bias=b1[:, m:m + 1]).then_inc(mlp_taken[half], 1)

            def layer2(n, m):
                half = USE_L2[m] % 2
                act.wait_ge(l2_done, M2 * n + m + 1)
                nc.scalar.activation(h2T[:, m, :], ps_mlp[half][:, 0:COLS], ACT.Relu,
                                     bias=b2[:, m:m + 1]).then_inc(mlp_taken[half], 1)

            def turned_bank(j, t, k):
                take_turned(act, nc.scalar.copy, j, t, k)

            def dots_unit(j, t, u):
                take_dots(act, nc.scalar.copy, j, t, u)

            def high_part(x):
                act.wait_ge(masked, x + 1)
                nc.scalar.copy(table[x][0:OH_P, :, 0, :], high[x % 2][0:OH_P, :, :]).then_inc(high_ready, 1)

            def second_half(j, mlp, ahead):
                if ahead:
                    take_spread(j + 1, 0)
                turned_bank(j, 1, 0)
                dots_unit(j, 0, 0)
                dots_unit(j, 0, 2)
                for k in range(2, NB, 2):
                    dots_unit(j, 0, k + 2)
                    if mlp and k == 2:
                        layer1(j - 1, 0)
                    turned_bank(j, 1, k)
                if mlp:
                    layer1(j - 1, 1)
                dots_unit(j, 1, 0)
                if mlp and ahead:
                    layer1(j - 1, 2)
                dots_unit(j, 1, 2)
                if mlp and ahead:
                    layer1(j - 1, 3)
                if ahead:
                    take_spread(j + 1, 1)
                dots_unit(j, 1, 4)
                if mlp and ahead:
                    layer2(j - 1, 0)
                    layer2(j - 1, 1)
                dots_unit(j, 1, 6)

            def pair(j):
                act.wait_ge(dotted[1], dots_until(j, 0))
                take_picked(j, 0)
                turned_bank(j, 0, 0)
                take_spread(j, 2)
                take_picked(j, 1)
                take_spread(j, 3)
                turned_bank(j, 0, 2)
                take_picked(j, 2)
                turned_bank(j, 0, 4)
                take_picked(j, 3)

            take_spread(0, 0)
            take_spread(0, 1)
            high_part(0)
            take_spread(0, 2)
            take_spread(0, 3)
            for x in range(1, len(OH_FEATS)):
                high_part(x)
                if x - 1 < NB:
                    turned_bank(0, 0, x - 1)
                if x in LAST_TABLES and x != LAST_TABLES[-1]:
                    take_picked(0, LAST_TABLES.index(x))
            take_picked(0, STEPS - 1)
            act.wait_ge(bias_loaded, 16 * (M1 + M2))
            second_half(0, False, True)
            with act.Fori(1, PAIRS - 1) as j:
                pair(j)
                second_half(j, True, True)
            pair(PAIRS - 1)
            second_half(PAIRS - 1, True, False)
            for m in range(2, M1):
                layer1(PAIRS - 2, m)
            for m in range(M2):
                layer2(PAIRS - 2, m)
            for m in range(M1):
                layer1(PAIRS - 1, m, LAST_BANKS[m])
            for m in range(M2):
                layer2(PAIRS - 1, m)

        @block.vector
        def _(dve):
            dve.wait_ge(ident_ready, 1)
            nc.vector.tensor_copy(ident16[:, :], ident[:, :]).then_inc(ident16_ready, 1)
            dve.wait_ge(row_ids_made, 1)
            nc.vector.tensor_copy(row_idsf[:, :], row_ids[:, :]).then_inc(row_ids_ready, 1)
            dve.wait_ge(ids_all_loaded, 16)
            nc.vector.tensor_copy(ids16[:, :, :], ids_all[:, :, :]).then_inc(ids16_ready, 1)
            dve.wait_ge(row_ids_ready, 1)

            def one_onehot(j, x):
                step, i = divmod(x, 2)
                dve.wait_ge(spread_taken, STEPS * j + step + 1)
                wait_if(dve, table_done, len(OH_FEATS) * j + before_in_buffer(x) + 1)
                for c in range(CHUNKS):
                    last = nc.vector.tensor_scalar(onehot[x % BUFS][0:OH_P, c, :], spread[step][0:OH_P, i, :],
                                                   row_idsf[0:OH_P, c:c + 1], None, ALU.is_equal)
                last.then_inc(onehot_ready, 1)

            def take_dense(n, out=zT):
                dve.wait_ge(dense_turned, n + 1)
                nc.vector.tensor_copy(out[0:DENSE, DENSE_CHUNK, :].rearrange("k (s t q) -> k t q s", s=SPM, t=TILES),
                                      ps_mlp[0][0:DENSE, 0:COLS].rearrange("k (t q s) -> k t q s", t=TILES, s=SPM),
                                      ).then_inc(mlp_taken[0], 1)

            def take_y(n):
                dve.wait_ge(l3_done, n + 1)
                nc.vector.tensor_copy(y[:, bass.ds(n * COLS, COLS)].rearrange("o (q s t) -> o s t q", s=SPM, t=TILES),
                                      ps_mlp[1][0:1, 0:COLS].rearrange("o (s t q) -> o s t q", s=SPM, t=TILES),
                                      ).then_inc(mlp_taken[1], 1)

            def turned_bank(j, t, k):
                take_turned(dve, nc.vector.tensor_copy, j, t, k)

            def dots_unit(j, t, u):
                take_dots(dve, nc.vector.tensor_copy, j, t, u)

            def split(x):
                dve.wait_ge(raw_loaded[x], 16)
                if x >= 2:
                    dve.wait_ge(high_ready, x - 1)
                source = raw[x % len(raw)][0:OH_P, :, :]
                nc.vector.tensor_scalar(high[x % 2][0:OH_P, :, :].bitcast(U32), source.bitcast(U32), HIGH_MASK, None,
                                        ALU.bitwise_and).then_inc(masked, 1)
                dve.wait_ge(masked, x + 1)
                nc.vector.tensor_tensor(table[x][0:OH_P, :, 1, :], source, high[x % 2][0:OH_P, :, :],
                                        ALU.subtract).then_inc(low_ready, 1)

            def second_half(j, mlp, ahead):
                turned_bank(j, 1, 1)
                dots_unit(j, 0, 1)
                if ahead:
                    one_onehot(j + 1, 0)
                dots_unit(j, 0, 3)
                if ahead:
                    one_onehot(j + 1, 1)
                dots_unit(j, 0, 5)
                turned_bank(j, 1, 3)
                dots_unit(j, 0, 7)
                for u in range(1, UNITS, 2):
                    if ahead and u == UNITS - 1:
                        one_onehot(j + 1, 2)
                    dots_unit(j, 1, u)
                if ahead:
                    one_onehot(j + 1, 3)
                if mlp and ahead:
                    take_y(j - 1)

            def pair(j):
                one_onehot(j, 4)
                one_onehot(j, 5)
                turned_bank(j, 0, 1)
                one_onehot(j, 6)
                one_onehot(j, 7)
                turned_bank(j, 0, 3)
                take_dense(j - 1)

            for x in range(len(OH_FEATS)):
                split(x)
                one_onehot(0, x)
            second_half(0, False, True)
            with dve.Fori(1, PAIRS - 1) as j:
                pair(j)
                second_half(j, True, True)
            pair(PAIRS - 1)
            second_half(PAIRS - 1, False, False)
            take_y(PAIRS - 2)
            take_dense(PAIRS - 1, z_lastT)
            take_y(PAIRS - 1)

        @block.tensor
        def _(pe):
            def spread_ids(j, step):
                wait_if(pe, spread_taken, STEPS * j + step)
                for i, f in enumerate(ONEHOT[step]):
                    for t in range(TILES):
                        at = (i * TILES + t) * P
                        one = ids16[:, bass.ds(j, 1), t * FEATS + f].to_broadcast([P, P])
                        last = nc.tensor.matmul(ps_spread[:, at:at + P], one, ident16[:, :], start=True, stop=True)
                last.then_inc(spread_done, 1)

            def pick(j, x):
                step, i = divmod(x, 2)
                if i == 0:
                    wait_if(pe, pick_taken, STEPS * j + step)
                pe.wait_ge(onehot_ready, len(OH_FEATS) * j + x + 1)
                if isinstance(j, int):
                    for part_ready in (high_ready, low_ready):
                        pe.wait_ge(part_ready, x + 1)
                for c in range(CHUNKS):
                    for part in range(PARTS):
                        last = nc.tensor.matmul(ps_pick[:, i * COLS:(i + 1) * COLS], table[x][0:OH_P, c, part, :],
                                                onehot[x % BUFS][0:OH_P, c, :], start=(c == 0 and part == 0),
                                                stop=(c == CHUNKS - 1 and part == PARTS - 1))
                last.then_inc(table_done, 1)

            def turn(j, t, k):
                half = turn_half(t, k)
                pe.wait_ge(gathered[t][k], 16 * len(BANKS[k]) * (j + 1))
                wait_if(pe, turn_taken[half], turns_before(j, t, k))
                for i, f in enumerate(BANKS[k]):
                    last = nc.tensor.transpose(ps_turn[half][:, i * P:(i + 1) * P],
                                               rows[t][:, GATHERED.index(f), :], ident[:, :])
                last.then_inc(turned[half], 1)

            def dot(j, t, u):
                if u == 0:
                    for half in range(2):
                        pe.wait_ge(turn_taken[half], turns_of(j, t, half))
                    pe.wait_ge(pick_taken, STEPS * (j + 1))
                wait_if(pe, dot_taken[u % 2], dots_until(j, t) + u // 2)
                for m in range(MPU):
                    q = u * MPU + m
                    left = embT[:, t, q * SPM:(q + 1) * SPM, :].rearrange("d s f -> d (s f)")[:, 0:M_DOT]
                    right = embT[:, t, q * SPM:(q + 1) * SPM, 1:FEATS]
                    last = nc.tensor.matmul(ps_dot[u % 2][0:M_DOT, m * P:m * P + SPM * PJ], left, right, start=True, stop=True)
                last.then_inc(dotted[u % 2], 1)

            def turn_dense(n):
                pe.wait_ge(dense_loaded, 16 * (n + 1))
                for t in range(TILES):
                    last = nc.tensor.transpose(ps_mlp[0][0:DENSE, t * P:(t + 1) * P], dense[:, t, :], ident[:, :])
                last.then_inc(dense_turned, 1)

            def layer1(n, m):
                half = USE_L1[m] % 2
                if m == 0:
                    pe.wait_ge(z_loaded, 16 * len(Z_PLACES) * (n + 1))
                    pe.wait_ge(mlp_taken[0], mlp_before(n, 0) + 1)
                else:
                    pe.wait_ge(mlp_taken[half], mlp_before(n, USE_L1[m]))
                for c, k in enumerate(KROWS):
                    last = nc.tensor.matmul(ps_mlp[half][:, 0:COLS], w1[0:k, c, m * P:(m + 1) * P], zT[0:k, c, :],
                                            start=(c == 0), stop=(c == len(KROWS) - 1))
                last.then_inc(l1_done, 1)

            def layer1_last(c):
                pe.wait_ge(z_last_loaded[c], 16 * len(BLOCKS[c]))
                if c == DENSE_CHUNK:
                    pe.wait_ge(mlp_taken[0], mlp_before(PAIRS - 1, 0) + 1)
                k = KROWS[c]
                for m in range(M1):
                    last = nc.tensor.matmul(LAST_BANKS[m][:, 0:COLS], w1[0:k, c, m * P:(m + 1) * P],
                                            z_lastT[0:k, c, :], start=(c == 0), stop=(c == len(KROWS) - 1))
                    if c == len(KROWS) - 1:
                        last.then_inc(l1_done, 1)

            def layer2(n, m):
                half = USE_L2[m] % 2
                for c in range(M1):
                    if m == 0 and c != 2:
                        use = USE_L1[max(c, 2) if c != 1 else 1]
                        pe.wait_ge(mlp_taken[use % 2], mlp_before(n, use) + 1)
                    last = nc.tensor.matmul(ps_mlp[half][:, 0:COLS], w2[:, c, m * P:(m + 1) * P], h1T[:, c, :],
                                            start=(c == 0), stop=(c == M1 - 1))
                last.then_inc(l2_done, 1)

            def layer3(n):
                for c in range(M2):
                    pe.wait_ge(mlp_taken[USE_L2[c] % 2], mlp_before(n, USE_L2[c]) + 1)
                    last = nc.tensor.matmul(ps_mlp[USE_L3 % 2][0:1, 0:COLS], w3[:, c:c + 1], h2T[:, c, :],
                                            start=(c == 0), stop=(c == M2 - 1))
                last.then_inc(l3_done, 1)

            def second_half(j, mlp, ahead):
                if ahead:
                    spread_ids(j + 1, 0)
                turn(j, 1, 0)
                turn(j, 1, 1)
                for u in range(4):
                    dot(j, 0, u)
                for k in range(2, NB):
                    dot(j, 0, k + 2)
                    if mlp and k == 2:
                        layer1(j - 1, 0)
                    if ahead and k in (3, 4):
                        pick(j + 1, k - 3)
                    turn(j, 1, k)
                dot(j, 0, 7)
                if mlp:
                    layer1(j - 1, 1)
                dot(j, 1, 0)
                dot(j, 1, 1)
                if mlp and ahead:
                    layer1(j - 1, 2)
                dot(j, 1, 2)
                if mlp and ahead:
                    layer1(j - 1, 3)
                dot(j, 1, 3)
                if ahead:
                    spread_ids(j + 1, 1)
                dot(j, 1, 4)
                if mlp and ahead:
                    layer2(j - 1, 0)
                dot(j, 1, 5)
                if mlp and ahead:
                    layer2(j - 1, 1)
                dot(j, 1, 6)
                dot(j, 1, 7)
                if mlp and ahead:
                    layer3(j - 1)

            def pair(j):
                turn(j, 0, 0)
                spread_ids(j, 2)
                pick(j, 2)
                pick(j, 3)
                turn(j, 0, 1)
                spread_ids(j, 3)
                turn(j, 0, 2)
                pick(j, 4)
                pick(j, 5)
                turn(j, 0, 3)
                turn(j, 0, 4)
                turn_dense(j - 1)
                pick(j, 6)
                pick(j, 7)

            pe.wait_ge(ident_ready, 1)
            pe.wait_ge(ident16_ready, 1)
            pe.wait_ge(ids16_ready, 1)
            for step in range(STEPS):
                spread_ids(0, step)
            for x in range(len(OH_FEATS)):
                pick(0, x)
                if x < NB:
                    turn(0, 0, x)
            second_half(0, False, True)
            pe.wait_ge(w1_loaded, 16 * W1_LOADS)
            pe.wait_ge(w2_loaded, 16)
            pe.wait_ge(w3_loaded, 16 * M2)
            with pe.Fori(1, PAIRS - 1) as j:
                pair(j)
                second_half(j, True, True)
            pair(PAIRS - 1)
            second_half(PAIRS - 1, True, False)
            for m in range(2, M1):
                layer1(PAIRS - 2, m)
            for m in range(M2):
                layer2(PAIRS - 2, m)
            layer1_last(0)
            layer3(PAIRS - 2)
            turn_dense(PAIRS - 1)
            for c in range(1, len(KROWS)):
                layer1_last(c)
            for m in range(M2):
                layer2(PAIRS - 1, m)
            layer3(PAIRS - 1)


_INS = ["dense_ctx", "ids"] + [f"tbl_{f}" for f in range(FEATS)] + ["W_top1", "b_top1", "W_top2", "b_top2", "W_top3"]


def kernel(**inputs):
    import numpy as _np
    import concourse.bacc as _bacc
    from concourse import mybir as _mybir
    from concourse.bass_utils import run_bass_kernel_spmd as _run

    nc = _bacc.Bacc("TRN2", target_bir_lowering=False, num_devices=1)
    arrays, aps = {}, {}
    for name in _INS:
        a = _np.ascontiguousarray(inputs[name])
        arrays[f"in_{name}_dram"] = a
        aps[name] = nc.dram_tensor(f"in_{name}_dram", a.shape, _mybir.dt.from_np(a.dtype), kind="ExternalInput").ap()
    z = nc.dram_tensor("z_dram", (PAIRS, PJ * I_ROWS * COLS), _mybir.dt.float32).ap()
    y = nc.dram_tensor("out_0_dram", (BATCH, 1), _mybir.dt.float32, kind="ExternalOutput").ap()
    dlrm(nc, aps, z, y.rearrange("b o -> o b"))
    r = _run(nc, [arrays], core_ids=[0])
    return r.results[0]["out_0_dram"]
```

```python
from contextlib import ExitStack

import concourse.bass as bass
from concourse import mybir

F32 = mybir.dt.float32
F32R = mybir.dt.float32r
U32 = mybir.dt.uint32
I32 = mybir.dt.int32
ALU = mybir.AluOpType
ACT = mybir.ActivationFunctionType

P = 128
BATCH = 2048
FEATS = 27
DIM = 128
DENSE = 16
HID1, HID2 = 512, 256
TILES = 2
COLS = TILES * P
PAIRS = BATCH // COLS

ONEHOT = [[3, 4], [9, 15], [19, 20], [6, 21]]
STEPS = len(ONEHOT)
LAST_TABLES = [2 * i + len(step) - 1 for i, step in enumerate(ONEHOT)]
OH_FEATS = [f for step in ONEHOT for f in step]
OH_ROWS = 1000
CHUNKS = 8
OH_P = OH_ROWS // CHUNKS
PARTS = 2
HIGH_MASK = 0xFFFFF000
BUFS = 4

GATHERED = [f for f in range(FEATS) if f not in OH_FEATS]
NG = len(GATHERED)
FPB = 4
BANKS = [GATHERED[k:k + FPB] for k in range(0, NG, FPB)]
NB = len(BANKS)

SPM, MPU = 4, 4
GROUPS = P // SPM
UNITS = GROUPS // MPU
RUN = TILES * GROUPS
I_ROWS = FEATS - 1
M_DOT = (SPM - 1) * FEATS + I_ROWS
PJ = FEATS - 1

BLOCKS = [[26, 24, 14], [22, 20, 16, 6], [18, 12, 10, 8, 4, 2]]
FIRST = [0, 0, DENSE]
DENSE_CHUNK = len(FIRST) - 1
POOL_CHUNK = 1
KROWS = [first + sum(2 * r for r in chunk) for first, chunk in zip(FIRST, BLOCKS)]
Z_PLACES = [(r, c, FIRST[c] + sum(2 * x for x in chunk[:n]))
            for c, chunk in enumerate(BLOCKS) for n, r in enumerate(chunk)]
assert max(KROWS) <= P and sorted(r for r, _, _ in Z_PLACES) == list(range(2, FEATS, 2))
M1, M2 = HID1 // P, HID2 // P
USE_L1 = list(range(1, 1 + M1))
USE_L2 = list(range(1 + M1, 1 + M1 + M2))
USE_L3 = 1 + M1 + M2
MLP_USES = USE_L3 + 1
H1_WAITS = {0: 2, 1: 1, 3: 3}
W1_LOADS = 2 * len(Z_PLACES) + 1


def runs(feats):
    out = []
    for i, f in enumerate(feats):
        if out and f == out[-1][1] + out[-1][2]:
            out[-1][2] += 1
        else:
            out.append([i, f, 1])
    return out


def mlp_before(n, use):
    return MLP_USES // 2 * n + use // 2


def turn_half(t, k):
    return (NB * t + k) % 2


def turns_before(j, t, k):
    return NB * j + (NB * t + k) // 2


def turns_of(j, t, half):
    return NB * j + (NB * (t + 1) - 1 - half) // 2 + 1


def dots_until(j, t):
    return TILES * (UNITS // 2) * j + UNITS // 2 * t


def before_in_buffer(x):
    return x - BUFS if x >= BUFS else max(range(x, len(OH_FEATS), BUFS)) - len(OH_FEATS)


def wait_if(eng, sem, value):
    if isinstance(value, int) and value <= 0:
        return
    eng.wait_ge(sem, value)


def dlrm(nc, inp, z_dram, y_dram):
    with ExitStack() as ctx:
        def sb(name, shape, dt=F32):
            return ctx.enter_context(nc.sbuf_tensor(name, shape, dt))

        def bank(name):
            return ctx.enter_context(nc.psum_tensor(name, [P, 512], F32))

        def sem(name):
            return ctx.enter_context(nc.semaphore(name))

        ids = sb("ids", [P, TILES, FEATS], I32)
        rows = [sb(f"rows{t}", [P, NG, DIM]) for t in range(TILES)]
        embT = sb("embT", [P, TILES, P, FEATS])
        table = [sb(f"table{x}", [P, CHUNKS, PARTS, DIM], F32R) for x in range(len(OH_FEATS))]
        row_ids = sb("row_ids", [P, CHUNKS], I32)
        row_idsf = sb("row_idsf", [P, CHUNKS])
        spread = [sb(f"spread{i}", [P, len(step), COLS], I32) for i, step in enumerate(ONEHOT)]
        onehot = [sb(f"onehot{i}", [P, CHUNKS, COLS], F32R) for i in range(BUFS)]
        dots = sb("dots", [P, SPM * PJ, RUN])
        span = CHUNKS * DIM // RUN
        spans = [dots[:, i * span:(i + 1) * span, :].rearrange("p a b -> p (a b)")
                 .rearrange("p (c d) -> p c d", d=DIM) for i in range(SPM * PJ // span)]
        raw, high = spans[0:4], spans[4:6]
        zT = sb("zT", [P, len(KROWS), COLS])
        z_lastT = rows[0][:, 0:len(KROWS) * COLS // DIM, :].rearrange("p a d -> p (a d)").rearrange("p (k c) -> p k c", c=COLS)
        h1T = sb("h1T", [P, M1, COLS])
        h2T = sb("h2T", [P, M2, COLS])
        y = sb("y", [1, BATCH])
        ident = sb("ident", [P, P])
        dense = sb("dense", [P, TILES, DENSE])
        w1 = sb("w1", [P, len(KROWS), HID1])
        w2 = sb("w2", [P, M1, HID2])
        w3 = sb("w3", [P, M2])
        b1 = sb("b1", [P, M1])
        b2 = sb("b2", [P, M2])

        ps_turn = [bank(f"ps_turn{i}") for i in range(2)]
        ps_dot = [bank(f"ps_dot{i}") for i in range(2)]
        ps_mlp = [bank(f"ps_mlp{i}") for i in range(2)]
        ps_pick = [bank(f"ps_pick{i}") for i in range(2)]

        ids_loaded = [sem(f"ids_loaded{t}") for t in range(TILES)]
        rows_free = sem("rows_free")
        gathered = [[sem(f"gathered{t}_{k}") for k in range(NB)] for t in range(TILES)]
        turned = [sem(f"turned{i}") for i in range(2)]
        turn_taken = [sem(f"turn_taken{i}") for i in range(2)]
        raw_loaded = [sem(f"raw_loaded{x}") for x in range(len(OH_FEATS))]
        masked = sem("masked")
        high_ready = sem("high_ready")
        low_ready = sem("low_ready")
        table_done = sem("table_done")
        spread_loaded = [sem(f"spread_loaded{i}") for i in range(STEPS)]
        onehot_ready = sem("onehot_ready")
        pick_taken = sem("pick_taken")
        dotted = [sem(f"dotted{i}") for i in range(2)]
        dot_taken = [sem(f"dot_taken{i}") for i in range(2)]
        z_stored = sem("z_stored")
        z_loaded = sem("z_loaded")
        z_last_loaded = [sem(f"z_last_loaded{c}") for c in range(len(KROWS))]
        dense_loaded = sem("dense_loaded")
        dense_turned = sem("dense_turned")
        l1_done = sem("l1_done")
        l2_done = sem("l2_done")
        l3_done = sem("l3_done")
        mlp_taken = [sem(f"mlp_taken{i}") for i in range(2)]
        y_stored = sem("y_stored")
        ident_zero = sem("ident_zero")
        ident_ready = sem("ident_ready")
        row_ids_made = sem("row_ids_made")
        row_ids_ready = sem("row_ids_ready")
        w1_zero = sem("w1_zero")
        w1_loaded = sem("w1_loaded")
        w2_loaded = sem("w2_loaded")
        w3_loaded = sem("w3_loaded")
        bias_loaded = sem("bias_loaded")

        ids_v = inp["ids"].rearrange("(j p t) f -> j p t f", p=P, t=TILES)
        dense_v = inp["dense_ctx"].rearrange("(j p t) k -> j p t k", p=P, t=TILES)

        LAST_BANKS = [*ps_turn, *ps_pick]

        def dots_of(s):
            return dots[s * FEATS:s * FEATS + I_ROWS, s * PJ:(s + 1) * PJ, :]

        def z_view(j):
            return z_dram[j].rearrange("(j i c) -> i j c", i=I_ROWS, c=COLS)

        def load_last(eng, chunks):
            for r, c, at in Z_PLACES:
                if c in chunks:
                    eng.dma_start(z_lastT[at:at + 2 * r, c, :], z_view(PAIRS - 1)[0:r, r - 2:r, :],
                                  ).then_inc(z_last_loaded[c], 16)

        def load_spread(eng, j, step):
            eng.dma_start(spread[step][0:OH_P, :, :],
                          inp["ids_onehot"][j, 2 * step:2 * step + len(ONEHOT[step]), :].partition_broadcast(OH_P),
                          ).then_inc(spread_loaded[step], 16)

        block = ctx.enter_context(nc.Block())

        @block.gpsimd
        def _(pool):
            nc.gpsimd.memset(ident[:, :], 0.0).then_inc(ident_zero, 1)
            pool.wait_ge(ident_zero, 1)
            nc.gpsimd.affine_select(out=ident[:, :], in_=ident[:, :], compare_op=ALU.not_equal, fill=1.0,
                                    base=0, pattern=[[-1, P]], channel_multiplier=1).then_inc(ident_ready, 1)
            nc.gpsimd.iota(row_ids[:, :], pattern=[[1, CHUNKS]], base=0,
                           channel_multiplier=CHUNKS).then_inc(row_ids_made, 1)
            nc.gpsimd.memset(w1[:, :, :], 0.0).then_inc(w1_zero, 1)

            def gather_pair(j):
                for t in range(TILES):
                    pool.wait_ge(ids_loaded[t], 16 * (j + 1))
                    for k, feats in enumerate(BANKS):
                        if not isinstance(j, int):
                            pool.wait_ge(turned[turn_half(t, k)], turns_before(j - 1, t, k) + 1)
                            pool.sem_inc(rows_free, 1)
                        for f in feats:
                            nc.gpsimd.indirect_dma_start(
                                rows[t][:, GATHERED.index(f), :], None, inp[f"tbl_{f}"],
                                bass.IndirectOffsetOnAxis(ap=ids[:, t, f:f + 1], axis=0),
                            ).then_inc(gathered[t][k], 16)

            gather_pair(0)
            with pool.Fori(1, PAIRS) as j:
                gather_pair(j)
            pool.wait_ge(z_stored, 16 * SPM * (PAIRS - 1 + TILES))
            load_last(nc.gpsimd, [POOL_CHUNK])

        @block.sync
        def _(sp):
            def load_ids(j, t):
                sp.dma_start(ids[:, t, :], ids_v[j, :, t, :]).then_inc(ids_loaded[t], 16)

            def load_dense(j):
                wait_if(sp, dense_turned, j)
                sp.dma_start(dense[:, :, :], dense_v[j]).then_inc(dense_loaded, 16)

            def refill_ids(j, t):
                sp.wait_ge(turned[turn_half(t, NB - 1)], turns_before(j, t, NB - 1) + 1)
                load_ids(j + 1, t)

            def bounce(j):
                for i in range(2):
                    sp.wait_ge(dot_taken[i], dots_until(j, TILES))
                z = z_view(j)
                for s in range(SPM):
                    sp.dma_start(z[:, :, s * RUN:(s + 1) * RUN],
                                 dots_of(s)[:, :, :]).then_inc(z_stored, 16)
                sp.wait_ge(z_stored, 16 * SPM * (j + 1))
                for r, c, at in Z_PLACES:
                    sp.dma_start(zT[at:at + 2 * r, c, :], z[0:r, r - 2:r, :]).then_inc(z_loaded, 16)

            def bounce_last():
                z = z_view(PAIRS - 1)
                for t in range(TILES):
                    for i in range(2):
                        sp.wait_ge(dot_taken[i], dots_until(PAIRS - 1, t + 1))
                    for s in range(SPM):
                        at = s * RUN + t * GROUPS
                        sp.dma_start(z[:, :, at:at + GROUPS], dots_of(s)[:, :, t * GROUPS:(t + 1) * GROUPS],
                                     ).then_inc(z_stored, 16)
                sp.wait_ge(z_stored, 16 * SPM * (PAIRS - 1 + TILES))
                load_last(nc.sync, [c for c in range(len(KROWS)) if c != POOL_CHUNK])

            for t in range(TILES):
                load_ids(0, t)
            for x, f in enumerate(OH_FEATS):
                if x in (0, 2):
                    load_spread(nc.sync, 0, x // 2)
                if x >= len(raw):
                    sp.wait_ge(low_ready, x - len(raw) + 1)
                sp.dma_start(raw[x % len(raw)][0:OH_P, :, :],
                             inp[f"tbl_{f}"].rearrange("(p c) d -> p c d", c=CHUNKS)).then_inc(raw_loaded[x], 16)
                if x == 3:
                    for step in range(2, STEPS):
                        load_spread(nc.sync, 0, step)
                    load_dense(0)
            sp.wait_ge(w1_zero, 1)
            for r, c, at in Z_PLACES:
                for j in (r - 1, r):
                    first = at + j - (r - 1)
                    sp.dma_start(w1[first:first + 2 * j - 1:2, c, :],
                                 inp["W_top1"][j * (j - 1) // 2:j * (j - 1) // 2 + j, :]).then_inc(w1_loaded, 16)
            sp.dma_start(w1[0:DENSE, DENSE_CHUNK, :], inp["W_top1"][FEATS * PJ // 2:, :]).then_inc(w1_loaded, 16)
            refill_ids(0, 0)
            sp.dma_start(w2[:, :, :], inp["W_top2"].rearrange("(k p) n -> p k n", p=P)).then_inc(w2_loaded, 16)
            for m in range(M1):
                sp.dma_start(b1[:, m:m + 1], inp["b_top1"][m * P:(m + 1) * P].rearrange("(p o) -> p o", o=1)).then_inc(bias_loaded, 16)
            for m in range(M2):
                sp.dma_start(b2[:, m:m + 1], inp["b_top2"][m * P:(m + 1) * P].rearrange("(p o) -> p o", o=1)).then_inc(bias_loaded, 16)
                sp.dma_start(w3[:, m:m + 1], inp["W_top3"][m * P:(m + 1) * P, :]).then_inc(w3_loaded, 16)

            refill_ids(0, 1)
            bounce(0)
            with sp.Fori(1, PAIRS - 1) as j:
                for t in range(TILES):
                    refill_ids(j, t)
                load_dense(j)
                bounce(j)
            load_dense(PAIRS - 1)
            bounce_last()
            sp.wait_ge(mlp_taken[USE_L3 % 2], mlp_before(PAIRS - 1, USE_L3) + 1)
            sp.dma_start(y_dram, y[:, :]).then_inc(y_stored, 16)
            sp.wait_ge(y_stored, 16)

        def take_turned(eng, copy, j, t, k):
            half = turn_half(t, k)
            eng.wait_ge(turned[half], turns_before(j, t, k) + 1)
            for at, f, n in runs(BANKS[k]):
                last = copy(embT[:, t, :, f:f + n].rearrange("d p f -> d f p"),
                            ps_turn[half][:, at * P:(at + n) * P].rearrange("d (f p) -> d f p", f=n))
            last.then_inc(turn_taken[half], 1)

        def take_dots(eng, copy, j, t, u):
            half = u % 2
            if t == 0 and u < 2:
                wait_if(eng, z_stored, 16 * SPM * j)
            eng.wait_ge(dotted[half], dots_until(j, t) + u // 2 + 1)
            first = t * GROUPS + u * MPU
            last = copy(dots[0:M_DOT, :, first:first + MPU].rearrange("p c q -> p q c"),
                        ps_dot[half][0:M_DOT, :].rearrange("p (q c) -> p q c", q=MPU)[:, :, 0:SPM * PJ])
            last.then_inc(dot_taken[half], 1)

        @block.scalar
        def _(act):
            def next_spread(j, step):
                act.wait_ge(onehot_ready, len(OH_FEATS) * j + LAST_TABLES[step] + 1)
                load_spread(nc.scalar, j + 1, step)

            def take_picked(j, step):
                act.wait_ge(table_done, len(OH_FEATS) * j + LAST_TABLES[step] + 1)
                feats = ONEHOT[step]
                n = len(feats)
                by = feats[-1] - feats[0] if n > 1 else 1
                for t in range(TILES):
                    last = nc.scalar.copy(
                        embT[:, t, :, feats[0]:feats[-1] + 1:by].rearrange("d p f -> d f p"),
                        ps_pick[step % 2][:, 0:n * COLS].rearrange("d (f t p) -> d t f p", f=n, t=TILES)[:, t, :, :])
                last.then_inc(pick_taken, 1)

            def layer1(n, m, src=None):
                half = USE_L1[m] % 2
                act.wait_ge(l1_done, M1 * n + m + 1)
                nc.scalar.activation(h1T[:, m, :], (src or ps_mlp[half])[:, 0:COLS], ACT.Relu,
                                     bias=b1[:, m:m + 1]).then_inc(mlp_taken[half], 1)

            def layer2(n, m):
                half = USE_L2[m] % 2
                act.wait_ge(l2_done, M2 * n + m + 1)
                nc.scalar.activation(h2T[:, m, :], ps_mlp[half][:, 0:COLS], ACT.Relu,
                                     bias=b2[:, m:m + 1]).then_inc(mlp_taken[half], 1)

            def turned_bank(j, t, k):
                take_turned(act, nc.scalar.copy, j, t, k)

            def dots_unit(j, t, u):
                take_dots(act, nc.scalar.copy, j, t, u)

            def high_part(x):
                act.wait_ge(masked, x + 1)
                nc.scalar.copy(table[x][0:OH_P, :, 0, :], high[x % 2][0:OH_P, :, :]).then_inc(high_ready, 1)

            def second_half(j, mlp, ahead):
                turned_bank(j, 1, 0)
                dots_unit(j, 0, 0)
                if ahead:
                    next_spread(j, 3)
                dots_unit(j, 0, 2)
                for k in range(2, NB, 2):
                    dots_unit(j, 0, k + 2)
                    if mlp and k == 4:
                        layer1(j - 1, 0)
                    turned_bank(j, 1, k)
                if mlp and ahead:
                    layer1(j - 1, 1)
                dots_unit(j, 1, 0)
                if mlp and ahead:
                    layer1(j - 1, 2)
                dots_unit(j, 1, 2)
                if mlp and ahead:
                    layer1(j - 1, 3)
                dots_unit(j, 1, 4)
                if mlp and ahead:
                    layer2(j - 1, 0)
                    layer2(j - 1, 1)
                dots_unit(j, 1, 6)

            def first_half(j, ahead):
                act.wait_ge(dotted[1], dots_until(j, 0))
                take_picked(j, 0)
                turned_bank(j, 0, 0)
                if ahead:
                    next_spread(j, 0)
                take_picked(j, 1)
                if ahead:
                    next_spread(j, 1)
                turned_bank(j, 0, 2)
                if ahead:
                    next_spread(j, 2)
                take_picked(j, 2)
                turned_bank(j, 0, 4)
                take_picked(j, 3)

            high_part(0)
            for x in range(1, len(OH_FEATS)):
                high_part(x)
                if x - 1 < NB:
                    turned_bank(0, 0, x - 1)
                if x in LAST_TABLES[:-1]:
                    step = LAST_TABLES.index(x)
                    take_picked(0, step)
                    next_spread(0, step)
            take_picked(0, STEPS - 1)
            second_half(0, False, True)
            act.wait_ge(bias_loaded, 16 * (M1 + M2))
            with act.Fori(1, PAIRS - 1) as j:
                first_half(j, True)
                second_half(j, True, True)
            first_half(PAIRS - 1, False)
            second_half(PAIRS - 1, True, False)
            for m in range(1, M1):
                layer1(PAIRS - 2, m)
            for m in range(M2):
                layer2(PAIRS - 2, m)
            for m in range(M1):
                layer1(PAIRS - 1, m, LAST_BANKS[m])
            for m in range(M2):
                layer2(PAIRS - 1, m)

        @block.vector
        def _(dve):
            dve.wait_ge(row_ids_made, 1)
            nc.vector.tensor_copy(row_idsf[:, :], row_ids[:, :]).then_inc(row_ids_ready, 1)
            dve.wait_ge(row_ids_ready, 1)

            def one_onehot(j, x):
                step, i = divmod(x, 2)
                dve.wait_ge(spread_loaded[step], 16 * (j + 1))
                wait_if(dve, table_done, len(OH_FEATS) * j + before_in_buffer(x) + 1)
                for c in range(CHUNKS):
                    last = nc.vector.tensor_scalar(onehot[x % BUFS][0:OH_P, c, :], spread[step][0:OH_P, i, :],
                                                   row_idsf[0:OH_P, c:c + 1], None, ALU.is_equal)
                last.then_inc(onehot_ready, 1)

            def take_dense(n, out=zT):
                dve.wait_ge(dense_turned, n + 1)
                nc.vector.tensor_copy(out[0:DENSE, DENSE_CHUNK, :].rearrange("k (s t q) -> k t q s", s=SPM, t=TILES),
                                      ps_mlp[0][0:DENSE, 0:COLS].rearrange("k (t q s) -> k t q s", t=TILES, s=SPM),
                                      ).then_inc(mlp_taken[0], 1)

            def take_y(n):
                dve.wait_ge(l3_done, n + 1)
                nc.vector.tensor_copy(y[:, bass.ds(n * COLS, COLS)].rearrange("o (q s t) -> o s t q", s=SPM, t=TILES),
                                      ps_mlp[1][0:1, 0:COLS].rearrange("o (s t q) -> o s t q", s=SPM, t=TILES),
                                      ).then_inc(mlp_taken[1], 1)

            def turned_bank(j, t, k):
                take_turned(dve, nc.vector.tensor_copy, j, t, k)

            def dots_unit(j, t, u):
                take_dots(dve, nc.vector.tensor_copy, j, t, u)

            def split(x):
                dve.wait_ge(raw_loaded[x], 16)
                if x >= 2:
                    dve.wait_ge(high_ready, x - 1)
                source = raw[x % len(raw)][0:OH_P, :, :]
                nc.vector.tensor_scalar(high[x % 2][0:OH_P, :, :].bitcast(U32), source.bitcast(U32), HIGH_MASK, None,
                                        ALU.bitwise_and).then_inc(masked, 1)
                dve.wait_ge(masked, x + 1)
                nc.vector.tensor_tensor(table[x][0:OH_P, :, 1, :], source, high[x % 2][0:OH_P, :, :],
                                        ALU.subtract).then_inc(low_ready, 1)

            def second_half(j, mlp, ahead):
                turned_bank(j, 1, 1)
                dots_unit(j, 0, 1)
                dots_unit(j, 0, 3)
                if ahead:
                    one_onehot(j + 1, 1)
                dots_unit(j, 0, 5)
                if ahead:
                    one_onehot(j + 1, 2)
                turned_bank(j, 1, 3)
                if ahead:
                    one_onehot(j + 1, 3)
                dots_unit(j, 0, 7)
                dots_unit(j, 1, 1)
                if ahead:
                    one_onehot(j + 1, 4)
                dots_unit(j, 1, 3)
                if ahead:
                    one_onehot(j + 1, 5)
                dots_unit(j, 1, 5)
                dots_unit(j, 1, 7)
                if mlp and ahead:
                    take_y(j - 1)

            def first_half(j, ahead):
                turned_bank(j, 0, 1)
                one_onehot(j, 6)
                one_onehot(j, 7)
                turned_bank(j, 0, 3)
                take_dense(j - 1)
                if ahead:
                    one_onehot(j + 1, 0)

            for x in range(len(OH_FEATS)):
                split(x)
                one_onehot(0, x)
            one_onehot(1, 0)
            second_half(0, False, True)
            with dve.Fori(1, PAIRS - 1) as j:
                first_half(j, True)
                second_half(j, True, True)
            first_half(PAIRS - 1, False)
            second_half(PAIRS - 1, False, False)
            take_y(PAIRS - 2)
            take_dense(PAIRS - 1, z_lastT)
            take_y(PAIRS - 1)

        @block.tensor
        def _(pe):
            def pick(j, x):
                step, i = divmod(x, 2)
                if i == 0:
                    wait_if(pe, pick_taken, STEPS * j + step - 1)
                pe.wait_ge(onehot_ready, len(OH_FEATS) * j + x + 1)
                if isinstance(j, int):
                    for part_ready in (high_ready, low_ready):
                        pe.wait_ge(part_ready, x + 1)
                for c in range(CHUNKS):
                    for part in range(PARTS):
                        last = nc.tensor.matmul(ps_pick[step % 2][:, i * COLS:(i + 1) * COLS], table[x][0:OH_P, c, part, :],
                                                onehot[x % BUFS][0:OH_P, c, :], start=(c == 0 and part == 0),
                                                stop=(c == CHUNKS - 1 and part == PARTS - 1))
                last.then_inc(table_done, 1)

            def turn(j, t, k):
                half = turn_half(t, k)
                pe.wait_ge(gathered[t][k], 16 * len(BANKS[k]) * (j + 1))
                wait_if(pe, turn_taken[half], turns_before(j, t, k))
                for i, f in enumerate(BANKS[k]):
                    last = nc.tensor.transpose(ps_turn[half][:, i * P:(i + 1) * P],
                                               rows[t][:, GATHERED.index(f), :], ident[:, :])
                last.then_inc(turned[half], 1)

            def dot(j, t, u):
                if u == 0:
                    for half in range(2):
                        pe.wait_ge(turn_taken[half], turns_of(j, t, half))
                    pe.wait_ge(pick_taken, STEPS * (j + 1))
                wait_if(pe, dot_taken[u % 2], dots_until(j, t) + u // 2)
                for m in range(MPU):
                    q = u * MPU + m
                    left = embT[:, t, q * SPM:(q + 1) * SPM, :].rearrange("d s f -> d (s f)")[:, 0:M_DOT]
                    right = embT[:, t, q * SPM:(q + 1) * SPM, 1:FEATS]
                    last = nc.tensor.matmul(ps_dot[u % 2][0:M_DOT, m * P:m * P + SPM * PJ], left, right, start=True, stop=True)
                last.then_inc(dotted[u % 2], 1)

            def turn_dense(n):
                pe.wait_ge(dense_loaded, 16 * (n + 1))
                for t in range(TILES):
                    last = nc.tensor.transpose(ps_mlp[0][0:DENSE, t * P:(t + 1) * P], dense[:, t, :], ident[:, :])
                last.then_inc(dense_turned, 1)

            def layer1(n, m):
                half = USE_L1[m] % 2
                if m == 0:
                    pe.wait_ge(z_loaded, 16 * len(Z_PLACES) * (n + 1))
                    pe.wait_ge(mlp_taken[0], mlp_before(n, 0) + 1)
                else:
                    pe.wait_ge(mlp_taken[half], mlp_before(n, USE_L1[m]))
                for c, k in enumerate(KROWS):
                    last = nc.tensor.matmul(ps_mlp[half][:, 0:COLS], w1[0:k, c, m * P:(m + 1) * P], zT[0:k, c, :],
                                            start=(c == 0), stop=(c == len(KROWS) - 1))
                last.then_inc(l1_done, 1)

            def layer1_last(c):
                pe.wait_ge(z_last_loaded[c], 16 * len(BLOCKS[c]))
                if c == DENSE_CHUNK:
                    pe.wait_ge(mlp_taken[0], mlp_before(PAIRS - 1, 0) + 1)
                k = KROWS[c]
                for m in range(M1):
                    last = nc.tensor.matmul(LAST_BANKS[m][:, 0:COLS], w1[0:k, c, m * P:(m + 1) * P],
                                            z_lastT[0:k, c, :], start=(c == 0), stop=(c == len(KROWS) - 1))
                    if c == len(KROWS) - 1:
                        last.then_inc(l1_done, 1)

            def layer2(n, m):
                half = USE_L2[m] % 2
                for c in range(M1):
                    if m == 0 and c in H1_WAITS:
                        use = USE_L1[H1_WAITS[c]]
                        pe.wait_ge(mlp_taken[use % 2], mlp_before(n, use) + 1)
                    last = nc.tensor.matmul(ps_mlp[half][:, 0:COLS], w2[:, c, m * P:(m + 1) * P], h1T[:, c, :],
                                            start=(c == 0), stop=(c == M1 - 1))
                last.then_inc(l2_done, 1)

            def layer3(n):
                for c in range(M2):
                    pe.wait_ge(mlp_taken[USE_L2[c] % 2], mlp_before(n, USE_L2[c]) + 1)
                    last = nc.tensor.matmul(ps_mlp[USE_L3 % 2][0:1, 0:COLS], w3[:, c:c + 1], h2T[:, c, :],
                                            start=(c == 0), stop=(c == M2 - 1))
                last.then_inc(l3_done, 1)

            def second_half(j, mlp, ahead):
                turn(j, 1, 0)
                turn(j, 1, 1)
                for u in range(4):
                    dot(j, 0, u)
                for k in range(2, NB):
                    dot(j, 0, k + 2)
                    if mlp and k == 4:
                        layer1(j - 1, 0)
                    if ahead and k in (3, 4):
                        pick(j + 1, k - 3)
                    turn(j, 1, k)
                dot(j, 0, 7)
                if mlp and ahead:
                    layer1(j - 1, 1)
                dot(j, 1, 0)
                dot(j, 1, 1)
                if mlp and ahead:
                    layer1(j - 1, 2)
                dot(j, 1, 2)
                if mlp and ahead:
                    layer1(j - 1, 3)
                dot(j, 1, 3)
                dot(j, 1, 4)
                if mlp and ahead:
                    layer2(j - 1, 0)
                dot(j, 1, 5)
                if mlp and ahead:
                    layer2(j - 1, 1)
                dot(j, 1, 6)
                dot(j, 1, 7)
                if mlp and ahead:
                    layer3(j - 1)

            def first_half(j):
                turn(j, 0, 0)
                pick(j, 2)
                pick(j, 3)
                turn(j, 0, 1)
                turn(j, 0, 2)
                pick(j, 4)
                pick(j, 5)
                turn(j, 0, 3)
                turn(j, 0, 4)
                turn_dense(j - 1)
                pick(j, 6)
                pick(j, 7)

            pe.wait_ge(ident_ready, 1)
            for x in range(len(OH_FEATS)):
                pick(0, x)
                if x < NB:
                    turn(0, 0, x)
            second_half(0, False, True)
            pe.wait_ge(w1_loaded, 16 * W1_LOADS)
            pe.wait_ge(w2_loaded, 16)
            pe.wait_ge(w3_loaded, 16 * M2)
            with pe.Fori(1, PAIRS - 1) as j:
                first_half(j)
                second_half(j, True, True)
            first_half(PAIRS - 1)
            second_half(PAIRS - 1, True, False)
            for m in range(1, M1):
                layer1(PAIRS - 2, m)
            for m in range(M2):
                layer2(PAIRS - 2, m)
            layer3(PAIRS - 2)
            turn_dense(PAIRS - 1)
            for c in range(len(KROWS)):
                layer1_last(c)
            for m in range(M2):
                layer2(PAIRS - 1, m)
            layer3(PAIRS - 1)


_INS = ["dense_ctx", "ids", "ids_onehot"] + [f"tbl_{f}" for f in range(FEATS)] + ["W_top1", "b_top1", "W_top2", "b_top2", "W_top3"]


def kernel(**inputs):
    import numpy as _np
    import concourse.bacc as _bacc
    from concourse import mybir as _mybir
    from concourse.bass_utils import run_bass_kernel_spmd as _run

    nc = _bacc.Bacc("TRN2", target_bir_lowering=False, num_devices=1)
    arrays, aps = {}, {}
    ids = _np.asarray(inputs["ids"]).reshape(PAIRS, P, TILES, FEATS).transpose(0, 3, 2, 1)
    inputs["ids_onehot"] = ids.reshape(PAIRS, FEATS, COLS)[:, OH_FEATS]
    for name in _INS:
        a = _np.ascontiguousarray(inputs[name])
        arrays[f"in_{name}_dram"] = a
        aps[name] = nc.dram_tensor(f"in_{name}_dram", a.shape, _mybir.dt.from_np(a.dtype), kind="ExternalInput").ap()
    z = nc.dram_tensor("z_dram", (PAIRS, PJ * I_ROWS * COLS), _mybir.dt.float32).ap()
    y = nc.dram_tensor("out_0_dram", (BATCH, 1), _mybir.dt.float32, kind="ExternalOutput").ap()
    dlrm(nc, aps, z, y.rearrange("b o -> o b"))
    r = _run(nc, [arrays], core_ids=[0])
    return r.results[0]["out_0_dram"]
```
